# Optimizing a Trainium2 kernel written in Bass

```python
import numpy as np
import jax
import jax.numpy as jnp

def _softmax(x, axis=-1):
    return jax.nn.softmax(x, axis=axis)
def _gelu(x):
    return jax.nn.gelu(x, approximate=True)
def _silu(x):
    return jax.nn.silu(x)
def _sigmoid(x):
    return jax.nn.sigmoid(x)
def _layernorm(x, axis=-1, eps=1e-5):
    m = jnp.mean(x, axis=axis, keepdims=True)
    v = jnp.var(x, axis=axis, keepdims=True)
    return (x - m) / jnp.sqrt(v + eps)
def _scatter_add(tgt, idx, src, axis=0):
    return tgt.at[idx].add(src)
def _segment_sum(src, seg, n):
    return jax.ops.segment_sum(src, seg, n)

kernel_name = 'mk_conv_preact_d1_conv_nchw256_54c41c'

def setup_inputs(seed: int = 0):
    np.random.seed(seed)
    _w = jnp.asarray
    def _rec_inputs():
        import jax
        import jax.numpy as jnp
        _gk = jax.random.key(seed)
        x = -0.0003957 + 1 * jax.random.normal(jax.random.fold_in(_gk, 1), (64, 256, 28, 28), jnp.float32)
        return x
    x = _rec_inputs()
    def _L0_conv_setup():
        import jax, jax.numpy as jnp
        import numpy as np
        from jax import lax
        K = 8
        SCALE = 100.0

        @jax.custom_vjp
        def bin_w(x):
            return jnp.sign(x)

        def _bin_w_fwd(x):
            return (jnp.sign(x), None)

        def _bin_w_bwd(_, g):
            return (g,)
        bin_w.defvjp(_bin_w_fwd, _bin_w_bwd)

        @jax.custom_vjp
        def bin_a(x):
            return jnp.sign(x)

        def _bin_a_fwd(x):
            return (jnp.sign(x), x)

        def _bin_a_bwd(x, g):
            return (g * jnp.clip(2.0 - jnp.abs(2.0 * x), 0.0, None),)
        bin_a.defvjp(_bin_a_fwd, _bin_a_bwd)

        @jax.custom_vjp
        def sdp(m, z, rv):
            return (rv @ z)[0] + m

        def _sdp_fwd(m, z, rv):
            return ((rv @ z)[0] + m, rv)

        def _sdp_bwd(rv, g):
            grad_m = g
            grad_z = rv.T @ g[None, :] * np.sqrt(SCALE)
            return (grad_m, grad_z, jnp.zeros_like(rv))
        sdp.defvjp(_sdp_fwd, _sdp_bwd)

        def _forward(x, M, Z, alpha, rv):
            N = M.size
            m = M.reshape(N)
            z = Z.reshape(K, N)
            A = m * m + jnp.sum(z * z, axis=0) / SCALE
            inv = lax.rsqrt(A)
            m_used = m + lax.stop_gradient(m * inv - m)
            z_used = z + lax.stop_gradient(z * inv - z)
            w = sdp(m_used, z_used, rv)
            bw = bin_w(w).reshape(M.shape)
            ba = bin_a(x)
            out = lax.conv_general_dilated(ba, bw, window_strides=(1, 1), padding=((1, 1), (1, 1)), dimension_numbers=('NCHW', 'OIHW', 'NCHW'))
            return out * alpha
        key = jax.random.key(seed)
        k1, k2, k3, k4, k5 = jax.random.split(key, 5)
        x = jax.random.normal(k1, (64, 256, 28, 28), dtype=jnp.float32)
        M = jax.random.normal(k2, (256, 256, 3, 3), dtype=jnp.float32)
        Z = jax.random.normal(k3, (8, 256, 256, 3, 3), dtype=jnp.float32)
        alpha = jax.random.uniform(k4, (256, 1, 1), dtype=jnp.float32)
        rv = jax.random.normal(k5, (1, 8), dtype=jnp.float32) * np.float32(1.0 / np.sqrt(SCALE))
        return {'x': x, 'M': M, 'Z': Z, 'alpha': alpha, 'rv': rv}
    _L0_conv_all = _L0_conv_setup()
    _L0_conv_in = {k: v for k, v in _L0_conv_all.items() if k in ('M', 'Z', 'alpha', 'rv', )}
    del _L0_conv_all

    return {
        "x": x,
        "L0_conv_M": _L0_conv_in["M"],
        "L0_conv_Z": _L0_conv_in["Z"],
        "L0_conv_alpha": _L0_conv_in["alpha"],
        "L0_conv_rv": _L0_conv_in["rv"],
    }

def reference(x, L0_conv_M, L0_conv_Z, L0_conv_alpha, L0_conv_rv):
    import jax
    import jax.numpy as jnp
    def _L0_conv_ref(x, M, Z, alpha, rv):
        import jax, jax.numpy as jnp
        import numpy as np
        from jax import lax
        K = 8
        SCALE = 100.0

        @jax.custom_vjp
        def bin_w(x):
            return jnp.sign(x)

        def _bin_w_fwd(x):
            return (jnp.sign(x), None)

        def _bin_w_bwd(_, g):
            return (g,)
        bin_w.defvjp(_bin_w_fwd, _bin_w_bwd)

        @jax.custom_vjp
        def bin_a(x):
            return jnp.sign(x)

        def _bin_a_fwd(x):
            return (jnp.sign(x), x)

        def _bin_a_bwd(x, g):
            return (g * jnp.clip(2.0 - jnp.abs(2.0 * x), 0.0, None),)
        bin_a.defvjp(_bin_a_fwd, _bin_a_bwd)

        @jax.custom_vjp
        def sdp(m, z, rv):
            return (rv @ z)[0] + m

        def _sdp_fwd(m, z, rv):
            return ((rv @ z)[0] + m, rv)

        def _sdp_bwd(rv, g):
            grad_m = g
            grad_z = rv.T @ g[None, :] * np.sqrt(SCALE)
            return (grad_m, grad_z, jnp.zeros_like(rv))
        sdp.defvjp(_sdp_fwd, _sdp_bwd)

        def _forward(x, M, Z, alpha, rv):
            N = M.size
            m = M.reshape(N)
            z = Z.reshape(K, N)
            A = m * m + jnp.sum(z * z, axis=0) / SCALE
            inv = lax.rsqrt(A)
            m_used = m + lax.stop_gradient(m * inv - m)
            z_used = z + lax.stop_gradient(z * inv - z)
            w = sdp(m_used, z_used, rv)
            bw = bin_w(w).reshape(M.shape)
            ba = bin_a(x)
            out = lax.conv_general_dilated(ba, bw, window_strides=(1, 1), padding=((1, 1), (1, 1)), dimension_numbers=('NCHW', 'OIHW', 'NCHW'))
            return out * alpha
        return _forward(x, M, Z, alpha, rv)

    def _gn(v, G=32, eps=1e-5):
        B_, C_, H_, W_ = v.shape
        g = v.reshape(B_, G, C_ // G, H_, W_)
        m = jnp.mean(g, axis=(2, 3, 4), keepdims=True)
        s = jnp.var(g, axis=(2, 3, 4), keepdims=True)
        return ((g - m) / jnp.sqrt(s + eps)).reshape(v.shape)

    def _ln_c(v, eps=1e-6):
        m = jnp.mean(v, axis=1, keepdims=True)
        s = jnp.var(v, axis=1, keepdims=True)
        return (v - m) / jnp.sqrt(s + eps)

    def _ln_t(v, eps=1e-5):
        m = jnp.mean(v, axis=-1, keepdims=True)
        s = jnp.var(v, axis=-1, keepdims=True)
        return (v - m) / jnp.sqrt(s + eps)

    def _to_tokens(v):
        B_, C_, H_, W_ = v.shape
        return v.reshape(B_, C_, H_ * W_).transpose(0, 2, 1)
    def _from_tokens(t, like):
        B_, C_, H_, W_ = like.shape
        return t.transpose(0, 2, 1).reshape(B_, C_, H_, W_)

    x = x + _L0_conv_ref(_gn(x), L0_conv_M, L0_conv_Z, L0_conv_alpha, L0_conv_rv)
    return x


_drawn_inputs = setup_inputs


def setup_inputs(seed=0):
    import zlib

    import numpy as np

    out = dict(_drawn_inputs(seed))
    spreads = {}
    factors = {}
    for name, (base, spread) in spreads.items():
        noise = np.random.default_rng([zlib.crc32(name.encode()), seed]).standard_normal(out[name].shape)
        drawn = base * np.exp(spread * noise) if base else spread * noise
        out[name] = jnp.asarray(drawn.astype(out[name].dtype))
    for name, factor in factors.items():
        out[name] = (out[name] * factor).astype(out[name].dtype)
    return out
```

```python
from contextlib import ExitStack

import concourse.bass as bass
from concourse import mybir

P = 128
ALU = mybir.AluOpType
ACT = mybir.ActivationFunctionType
BF16 = mybir.dt.bfloat16
F32 = mybir.dt.float32

GROUPS = 32
GN_EPS = 1e-5
Z_SCALE = 100.0

BODY = 8
LOAD_LEAD = 6
STAT_LEAD = 4
GROUP_LEAD = 3
SIGN_LEAD = 2
POINT_LEAD = 1
SMALL = 4


def conv_preact(nc, x, M, Z, alpha, rv, out):
    N, C, H, W = x.shape
    K, CO, CI, KH, KW = Z.shape
    HALVES = C // P
    assert HALVES == 2 and CO == C and CI == C and N % BODY == 0 and KH == 3 and KW == 3
    PIX = H * W
    TR = H // 2
    HALF_PIX = TR * W
    PH, PW = H + 2, W + 2
    TAPS = KH * KW
    CB = 64
    CHUNKS_PER_HALF = CI // CB
    CHUNKS = HALVES * CHUNKS_PER_HALF
    CW = CB * TAPS
    CPG = C // GROUPS
    TILES = N * HALVES
    E12 = H
    PROWS = H + 2 * TR

    x_v = x.rearrange("n (h p) a b -> n p h (a b)", p=P)
    out_v = out.rearrange("n (h p) a b -> n p h (a b)", p=P)
    z_v = Z.rearrange("k o i a b -> o k (i a b)")
    m_v = M.rearrange("o i a b -> o (i a b)")
    alpha_v = alpha.rearrange("(h p) a b -> h p (a b)", p=P)

    with ExitStack() as ctx:
        def sb(name, shape, dt):
            return ctx.enter_context(nc.sbuf_tensor(name, shape, dt))

        def psum(name, shape, dt):
            return ctx.enter_context(nc.psum_tensor(name, shape, dt))

        def sem(name):
            return ctx.enter_context(nc.semaphore(name))

        x_sb = sb("x_sb", [P, BODY, HALVES, PIX], F32)
        signs = sb("signs", [P, 2, HALVES, PH * PW], BF16)
        points = sb("points", [P, SMALL, HALVES, PROWS, PW], BF16)
        u = sb("u", [P, HALVES, 4, KW, CO], BF16)
        z_sb = sb("z_sb", [P, 2, K, CW], F32)
        m_sb = sb("m_sb", [P, 2, CW], F32)
        z_sq = sb("z_sq", [P, K, CW], F32)
        m_sq = sb("m_sq", [P, 2, CW], F32)
        a_sum = sb("a_sum", [P, 2, CW], F32)
        root = sb("root", [P, 2, CW], F32)
        inv = sb("inv", [P, CW], F32)
        q = sb("q", [P, 2, CW], F32)
        w_sign = sb("w_sign", [P, 2, 2 * CW], BF16)
        g_half = sb("g_half", [P, 2, KH, P], BF16)
        g_sum = sb("g_sum", [P, 2, P], BF16)
        rv_sb = sb("rv_sb", [P, K], F32)
        alpha_sb = sb("alpha_sb", [P, HALVES], F32)
        alpha_neg = sb("alpha_neg", [P, HALVES], F32)
        alpha_two = sb("alpha_two", [P, HALVES], F32)
        ident = sb("ident", [P, P], BF16)
        avg_sums = sb("avg_sums", [P, P], F32)
        avg_means = sb("avg_means", [P, P], F32)
        unread = sb("unread", [P, 2, PIX], BF16)
        bn = sb("bn", [P, 2, 2, 6], F32)
        chan = sb("chan", [P, SMALL, 4], F32)
        grp = sb("grp", [P, SMALL, 4], F32)
        mean_sq = sb("mean_sq", [P, SMALL, 2], F32)
        var = sb("var", [P, SMALL, 2], F32)
        var_eps = sb("var_eps", [P, SMALL, 2], F32)
        std = sb("std", [P, SMALL, 2], F32)
        rstd = sb("rstd", [P, SMALL, 2], F32)
        shift = sb("shift", [P, SMALL, 2], F32)
        m1_two = sb("m1_two", [P, 2, HALF_PIX], F32)
        odd_part = sb("odd_part", [P, 2, HALF_PIX], F32)

        even_ps = [psum(f"even_ps{i}", [P, 512], F32) for i in range(4)]
        odd_ps = [psum(f"odd_ps{i}", [P, 512], F32) for i in range(2)]
        grp_ps = psum("grp_ps", [P, 512], F32)
        wt_ps = psum("wt_ps", [P, 1024], BF16)

        consts_loaded = sem("consts_loaded")
        z_loaded = [sem(f"z_loaded{i}") for i in range(2)]
        x_loaded = [sem(f"x_loaded{i}") for i in range(BODY)]
        stored = [sem(f"stored{i}") for i in range(BODY)]
        const_step = sem("const_step")
        borders_zero = sem("borders_zero")
        alpha_ready = sem("alpha_ready")
        pool_step = sem("pool_step")
        dve_step = sem("dve_step")
        squares_done = sem("squares_done")
        sq_sum_done = sem("sq_sum_done")
        q_done = sem("q_done")
        a_done = sem("a_done")
        root_done = sem("root_done")
        w_done = sem("w_done")
        w_sign_done = sem("w_sign_done")
        wt_done = sem("wt_done")
        g_done = sem("g_done")
        u_done = sem("u_done")
        act_sums_done = sem("act_sums_done")
        dve_sums_done = sem("dve_sums_done")
        grp_done = sem("grp_done")
        grp_copied = sem("grp_copied")
        var_done = sem("var_done")
        std_done = sem("std_done")
        rstd_step = sem("rstd_step")
        rstd_done = sem("rstd_done")
        signs_done = sem("signs_done")
        points_done = sem("points_done")
        m1_done = sem("m1_done")
        m2_done = sem("m2_done")
        m3_done = sem("m3_done")
        m0_done = sem("m0_done")
        m1_copied = sem("m1_copied")
        diff_done = sem("diff_done")
        odd_part_done = sem("odd_part_done")
        odd_out = sem("odd_out")
        even_out = sem("even_out")

        def need(eng, s, value):
            if not (isinstance(value, int) and value <= 0):
                eng.wait_ge(s, value)

        def rows_of(slot, h, parity):
            return x_sb[:, slot, h, :].rearrange("p (t r w) -> p t r w", r=2, w=W)[:, :, parity, :]

        block = ctx.enter_context(nc.Block())

        @block.sync
        def _(sp):
            sp.dma_start(rv_sb[:], rv.to_broadcast([P, K])).then_inc(consts_loaded, 16)
            for h in range(HALVES):
                sp.dma_start(alpha_sb[:, h:h + 1], alpha_v[h]).then_inc(consts_loaded, 16)

            def load_chunk(c):
                h, b = divmod(c, CHUNKS_PER_HALF)
                need(sp, q_done, c - 1)
                need(sp, squares_done, 2 * (c - 1))
                sp.dma_start(z_sb[:, c % 2], z_v[h * P:(h + 1) * P, :, b * CW:(b + 1) * CW]).then_inc(z_loaded[c % 2], 16)
                sp.dma_start(m_sb[:, c % 2], m_v[h * P:(h + 1) * P, b * CW:(b + 1) * CW]).then_inc(z_loaded[c % 2], 16)

            def load(i0, s, first):
                if not first:
                    sp.wait_ge(stored[s], i0 * 2)
                sp.dma_start(x_sb[:, s], x_v[i0 + s]).then_inc(x_loaded[s], 16)

            def store(i0, s):
                sp.wait_ge(odd_out, (i0 + s + 1) * HALVES)
                sp.wait_ge(even_out, (i0 + s + 1) * HALVES)
                sp.dma_start(out_v[i0 + s], x_sb[:, s]).then_inc(stored[s], 16)

            for c in range(CHUNKS):
                load_chunk(c)
                if c >= CHUNKS - STAT_LEAD:
                    load(0, c - (CHUNKS - STAT_LEAD), True)
            for s in range(STAT_LEAD, LOAD_LEAD):
                load(0, s, True)

            def body(i0, first, last):
                for s in range(BODY):
                    store(i0, s)
                    t = s + LOAD_LEAD
                    if t < BODY:
                        load(i0, t, first)
                    elif not last:
                        load(i0 + BODY, t - BODY, False)

            body(0, True, False)
            with sp.Fori(BODY, N - 2 * BODY + 1, BODY) as i0:
                body(i0, False, False)
            body(N - BODY, False, True)
            for s in range(BODY):
                sp.wait_ge(stored[s], 16 * (N // BODY))

        @block.tensor
        def _(pe):
            def transpose_weights():
                pe.wait_ge(const_step, 8)
                for g in range(HALVES * HALVES):
                    pe.wait_ge(w_sign_done, 2 * (g + 1))
                    v = w_sign[:, g % 2].rearrange("p (i a b) -> p a b i", a=KH, b=KW)
                    for kw in range(KW):
                        r = g * KW + kw
                        need(pe, g_done, 3 * r)
                        for kh in range(KH):
                            mm = pe.transpose(wt_ps[:, kh * P:(kh + 1) * P], v[:, kh, kw, :], ident[:])
                        mm.then_inc(wt_done, 1)

            def group(i, k):
                pe.wait_ge(act_sums_done, 2 * (i + 1))
                pe.wait_ge(dve_sums_done, i + 1)
                need(pe, grp_copied, i)
                pe.matmul(grp_ps[:, 0:2], avg_sums[:], chan[:, k % SMALL, 0:2], start=True, stop=True)
                pe.matmul(grp_ps[:, 2:4], avg_means[:], chan[:, k % SMALL, 2:4], start=True, stop=True).then_inc(grp_done, 1)

            def product(bank, point, row0, step, s, h, start, stop):
                for ch in range(HALVES):
                    for kw in range(KW):
                        e = points[:, s % SMALL, ch, row0:row0 + step * (TR - 1) + 1:step, kw:kw + W]
                        mm = pe.matmul(bank[:, 0:HALF_PIX], u[:, ch, point, kw, h * P:(h + 1) * P], e,
                                       start=start and ch == 0 and kw == 0,
                                       stop=stop and ch == HALVES - 1 and kw == KW - 1, skip_group_check=True)
                return mm

            def finish(t, k):
                s, h = divmod(k, HALVES)
                need(pe, odd_out, t - 1)
                product(odd_ps[k % 2], 3, 1, 2, s, h, True, True).then_inc(m3_done, 1)
                pe.wait_ge(diff_done, t + 1)
                product(even_ps[k % 4], 0, 0, 2, s, h, False, True).then_inc(m0_done, 1)

            transpose_weights()
            for i in range(GROUP_LEAD):
                group(i, i)
            pe.wait_ge(u_done, 2 * HALVES * HALVES * KW)
            pe.wait_ge(g_done, 3 * HALVES * HALVES * KW)

            def body(i0, first, last):
                for k in range(BODY * HALVES):
                    s, h = divmod(k, HALVES)
                    i, t = i0 + s, i0 * HALVES + k
                    if h == 0:
                        pe.wait_ge(points_done, (i + 1) * 3)
                    need(pe, even_out, t - 3)
                    product(even_ps[k % 4], 1, E12, 1, s, h, True, False).then_inc(m1_done, 1)
                    if not (first and k == 0):
                        finish(t - 1, (k - 1) % (BODY * HALVES))
                    pe.wait_ge(m1_copied, t + 1)
                    product(even_ps[k % 4], 2, E12 + TR, 1, s, h, False, False).then_inc(m2_done, 1)
                    if h == 0 and not (last and s + GROUP_LEAD >= BODY):
                        group(i + GROUP_LEAD, s + GROUP_LEAD)

            body(0, True, False)
            with pe.Fori(BODY, N - 2 * BODY + 1, BODY) as i0:
                body(i0, False, False)
            body(N - BODY, False, True)
            finish(TILES - 1, BODY * HALVES - 1)

        @block.scalar
        def _(act):
            def chunk_squares(c):
                act.wait_ge(z_loaded[c % 2], 32 * (c // 2 + 1))
                need(act, a_done, c)
                nc.scalar.activation(z_sq[:], z_sb[:, c % 2], ACT.Square).then_inc(squares_done, 1)
                nc.scalar.activation(m_sq[:, c % 2], m_sb[:, c % 2], ACT.Square).then_inc(squares_done, 1)

            def chunk_root(c):
                act.wait_ge(a_done, c + 1)
                need(act, w_done, c - 1)
                nc.scalar.activation(root[:, c % 2], a_sum[:, c % 2], ACT.Sqrt).then_inc(root_done, 1)

            def chunk_sign(c):
                act.wait_ge(w_done, c + 1)
                g = c // 2
                need(act, wt_done, KW * (g - 1))
                nc.scalar.activation(w_sign[:, g % 2, (c % 2) * CW:(c % 2 + 1) * CW], q[:, c % 2],
                                     ACT.Sign).then_inc(w_sign_done, 1)

            def copy_taps(r):
                g, kw = divmod(r, KW)
                h, ch = divmod(g, HALVES)
                act.wait_ge(wt_done, r + 1)
                need(act, u_done, 2 * (r - 1))
                nc.scalar.activation(g_half[:, r % 2], wt_ps[:, 0:KH * P].rearrange("p (a o) -> p a o", o=P),
                                     ACT.Copy, scale=0.5).then_inc(g_done, 1)
                nc.scalar.activation(u[:, ch, 0, kw, h * P:(h + 1) * P], wt_ps[:, 0:P], ACT.Copy).then_inc(g_done, 1)
                nc.scalar.activation(u[:, ch, 3, kw, h * P:(h + 1) * P], wt_ps[:, 2 * P:3 * P],
                                     ACT.Copy, scale=-1.0).then_inc(g_done, 1)

            def sums(i0, s):
                act.wait_ge(x_loaded[s], (i0 + BODY) * 2)
                need(act, act_sums_done, (i0 + s) * 2)
                nc.scalar.activation(unread[:, 0], x_sb[:, s, 0], ACT.Copy,
                                     accum_out=chan[:, s % SMALL, 0:1]).then_inc(act_sums_done, 1)
                nc.scalar.activation(unread[:, 1], x_sb[:, s, 0], ACT.Square,
                                     accum_out=chan[:, s % SMALL, 1:2]).then_inc(act_sums_done, 1)

            def copy_group(i, s):
                act.wait_ge(grp_done, i + 1)
                nc.scalar.activation(grp[:, s % SMALL], grp_ps[:, 0:4], ACT.Copy).then_inc(grp_copied, 1)

            def deviation(i, s):
                act.wait_ge(var_done, i + 1)
                nc.scalar.activation(std[:, s % SMALL], var_eps[:, s % SMALL], ACT.Sqrt).then_inc(std_done, 1)

            def image_signs(i, s):
                act.wait_ge(rstd_done, i + 1)
                need(act, points_done, 3 * (i - 1))
                for h in range(HALVES):
                    o = signs[:, s % 2, h].rearrange("p (a b) -> p a b", b=PW)[:, 1:H + 1, 1:W + 1]
                    nc.scalar.activation(o, x_sb[:, s, h].rearrange("p (a b) -> p a b", b=W), ACT.Sign,
                                         bias=shift[:, s % SMALL, h:h + 1],
                                         scale=rstd[:, s % SMALL, h:h + 1]).then_inc(signs_done, 1)

            for c in range(CHUNKS + 2):
                if c < CHUNKS:
                    chunk_squares(c)
                if 1 <= c <= CHUNKS:
                    chunk_root(c - 1)
                if c >= 2:
                    chunk_sign(c - 2)
                    if c % 2 == 1:
                        for kw in range(KW):
                            copy_taps((c - 3) // 2 * KW + kw)
            for s in range(STAT_LEAD):
                sums(0, s)
            for s in range(GROUP_LEAD):
                copy_group(s, s)
            for s in range(SIGN_LEAD):
                deviation(s, s)
            act.wait_ge(borders_zero, 1)
            for s in range(SIGN_LEAD):
                image_signs(s, s)
            act.wait_ge(alpha_ready, 2)

            def body(i0, first, last):
                def lead(f, s, ahead, groups=False):
                    if s + ahead < BODY or not last:
                        f(i0 + s + ahead, (s + ahead) % BODY)

                for k in range(BODY * HALVES):
                    s, h = divmod(k, HALVES)
                    t = i0 * HALVES + k
                    act.wait_ge(m1_done, t + 1)
                    need(act, diff_done, t - 1)
                    nc.scalar.activation(m1_two[:, k % 2], even_ps[k % 4][:, 0:HALF_PIX], ACT.Copy,
                                         scale=alpha_two[:, h:h + 1]).then_inc(m1_copied, 1)
                    if h == 0:
                        lead(deviation, s, SIGN_LEAD)
                        if s + STAT_LEAD < BODY:
                            sums(i0, s + STAT_LEAD)
                        elif not last:
                            sums(i0 + BODY, s + STAT_LEAD - BODY)
                    else:
                        lead(copy_group, s, GROUP_LEAD)
                        lead(image_signs, s, SIGN_LEAD)

            body(0, True, False)
            with act.Fori(BODY, N - 2 * BODY + 1, BODY) as i0:
                body(i0, False, False)
            body(N - BODY, False, True)

        @block.gpsimd
        def _(pool):
            made = [0]

            def after(ins):
                made[0] += 1
                ins.then_inc(const_step, 1)
                pool.wait_ge(const_step, made[0])

            after(nc.gpsimd.memset(ident[:], 0.0))
            after(nc.gpsimd.affine_select(out=ident[:], in_=ident[:], compare_op=ALU.not_equal, fill=1.0, base=0,
                                          pattern=[[-1, P]], channel_multiplier=1))
            for avg, value in ((avg_sums, 1.0 / (CPG * PIX)), (avg_means, 1.0 / CPG)):
                v = avg[:].rearrange("p (g c) -> p g c", c=CPG)
                after(nc.gpsimd.memset(avg[:], value))
                after(nc.gpsimd.affine_select(out=v, in_=v, compare_op=ALU.is_ge, fill=0.0, base=0,
                                              pattern=[[-CPG, P // CPG], [0, CPG]], channel_multiplier=1))
                after(nc.gpsimd.affine_select(out=v, in_=v, compare_op=ALU.is_ge, fill=0.0, base=CPG - 1,
                                              pattern=[[CPG, P // CPG], [0, CPG]], channel_multiplier=-1))
            nc.gpsimd.memset(signs[:], 0.0).then_inc(borders_zero, 1)

            steps = [0]

            def then(ins):
                steps[0] += 1
                ins.then_inc(pool_step, 1)
                pool.wait_ge(pool_step, steps[0])

            def chunk_sum(c):
                pool.wait_ge(squares_done, 2 * (c + 1))
                k = K // 2
                while k > 1:
                    then(nc.gpsimd.tensor_tensor(z_sq[:, 0:k], z_sq[:, 0:k], z_sq[:, k:2 * k], ALU.add))
                    k //= 2
                nc.gpsimd.tensor_tensor(z_sq[:, 0], z_sq[:, 0], z_sq[:, 1], ALU.add).then_inc(sq_sum_done, 1)

            def combine_taps(r):
                g, kw = divmod(r, KW)
                h, ch = divmod(g, HALVES)
                pool.wait_ge(g_done, 3 * r + 1)
                then(nc.gpsimd.tensor_tensor(g_sum[:, r % 2], g_half[:, r % 2, 0], g_half[:, r % 2, 2], ALU.add))
                for point, op in ((1, ALU.add), (2, ALU.subtract)):
                    nc.gpsimd.tensor_tensor(u[:, ch, point, kw, h * P:(h + 1) * P], g_sum[:, r % 2],
                                            g_half[:, r % 2, 1], op).then_inc(u_done, 1)

            for c in range(CHUNKS + 3):
                if c < CHUNKS:
                    chunk_sum(c)
                if c >= 3 and c % 2 == 1:
                    for kw in range(KW):
                        combine_taps((c - 3) // 2 * KW + kw)

            def variance(i, s, between=None):
                pool.wait_ge(grp_copied, i + 1)
                k = s % SMALL
                n = i * 2 + steps[0]
                mean = grp[:, k, 0:4:2]
                nc.gpsimd.tensor_tensor(mean_sq[:, k], mean, mean, ALU.mult).then_inc(pool_step, 1)
                pool.wait_ge(pool_step, n + 1)
                nc.gpsimd.tensor_tensor(var[:, k], grp[:, k, 1:4:2], mean_sq[:, k], ALU.subtract).then_inc(pool_step, 1)
                pool.wait_ge(pool_step, n + 2)
                if between:
                    between()
                nc.gpsimd.tensor_scalar(var_eps[:, k], var[:, k], 0.0, GN_EPS, ALU.max, ALU.add).then_inc(var_done, 1)

            def odd(t, k):
                s, h = divmod(k, HALVES)
                v = odd_part[:, k % 2].rearrange("p (a b) -> p a b", b=W)
                pool.wait_ge(diff_done, t + 1)
                nc.gpsimd.tensor_tensor(v, v, rows_of(s, h, 1), ALU.add).then_inc(odd_part_done, 1)

            for s in range(GROUP_LEAD):
                variance(s, s)

            def body(i0, first, last):
                for k in range(BODY * HALVES):
                    s, h = divmod(k, HALVES)

                    def odd_before():
                        if not (first and k == 0):
                            odd(i0 * HALVES + k - 1, (k - 1) % (BODY * HALVES))

                    if h == 1 and (s + GROUP_LEAD < BODY or not last):
                        variance(i0 + s + GROUP_LEAD, (s + GROUP_LEAD) % BODY, odd_before)
                    else:
                        odd_before()

            body(0, True, False)
            with pool.Fori(BODY, N - 2 * BODY + 1, BODY) as i0:
                body(i0, False, False)
            body(N - BODY, False, True)
            odd(TILES - 1, BODY * HALVES - 1)

        @block.vector
        def _(dve):
            steps = [0]

            def then(ins):
                steps[0] += 1
                ins.then_inc(dve_step, 1)
                dve.wait_ge(dve_step, steps[0])

            dve.wait_ge(consts_loaded, 16 * (1 + HALVES))
            nc.vector.tensor_scalar(alpha_neg[:], alpha_sb[:], -1.0, None, ALU.mult).then_inc(alpha_ready, 1)
            nc.vector.tensor_scalar(alpha_two[:], alpha_sb[:], 2.0, None, ALU.mult).then_inc(alpha_ready, 1)

            def chunk_q(c):
                dve.wait_ge(z_loaded[c % 2], 32 * (c // 2 + 1))
                need(dve, w_sign_done, c - 1)
                for k in range(K):
                    ins = nc.vector.scalar_tensor_tensor(
                        out=q[:, c % 2], in0=z_sb[:, c % 2, k], scalar=rv_sb[:, k:k + 1],
                        in1=m_sb[:, c % 2] if k == 0 else q[:, c % 2], op0=ALU.mult, op1=ALU.add)
                    if k < K - 1:
                        then(ins)
                ins.then_inc(q_done, 1)

            def chunk_a(c):
                dve.wait_ge(sq_sum_done, c + 1)
                need(dve, root_done, c - 1)
                nc.vector.scalar_tensor_tensor(out=a_sum[:, c % 2], in0=z_sq[:, 0], scalar=1.0 / Z_SCALE,
                                               in1=m_sq[:, c % 2], op0=ALU.mult, op1=ALU.add).then_inc(a_done, 1)

            def chunk_w(c):
                dve.wait_ge(root_done, c + 1)
                then(nc.vector.reciprocal(inv[:], root[:, c % 2]))
                dve.wait_ge(q_done, c + 1)
                nc.vector.tensor_tensor(q[:, c % 2], q[:, c % 2], inv[:], ALU.mult).then_inc(w_done, 1)

            for c in range(CHUNKS + 1):
                if c >= 1:
                    chunk_a(c - 1)
                if c < CHUNKS:
                    chunk_q(c)
                if c >= 1:
                    chunk_w(c - 1)

            def sums(i0, s, first_output=None, second_output=None):
                dve.wait_ge(x_loaded[s], (i0 + BODY) * 2)
                b, k = s % 2, s % SMALL
                n = (i0 + s) * 3 + steps_images
                for c in range(2):
                    nc.vector.bn_stats(bn[:, b, c], x_sb[:, s, 1, c * HALF_PIX:(c + 1) * HALF_PIX]).then_inc(dve_step, 1)
                dve.wait_ge(dve_step, n + 2)
                if first_output:
                    first_output()
                nc.vector.bn_aggr(chan[:, k, 2:4], bn[:, b].rearrange("p c k -> p (c k)")).then_inc(dve_step, 1)
                dve.wait_ge(dve_step, n + 3)
                if second_output:
                    second_output()
                nc.vector.scalar_tensor_tensor(out=chan[:, k, 3:4], in0=chan[:, k, 2:3],
                                               scalar=chan[:, k, 2:3], in1=chan[:, k, 3:4],
                                               op0=ALU.mult, op1=ALU.add).then_inc(dve_sums_done, 1)

            steps_images = steps[0]

            def reciprocal_std(i, s):
                dve.wait_ge(std_done, i + 1)
                k = s % SMALL
                nc.vector.reciprocal(rstd[:, k], std[:, k]).then_inc(rstd_step, 1)
                dve.wait_ge(rstd_step, i + 1)
                nc.vector.scalar_tensor_tensor(out=shift[:, k], in0=grp[:, k, 0:4:2], scalar=-1.0,
                                               in1=rstd[:, k], op0=ALU.mult, op1=ALU.mult).then_inc(rstd_done, 1)

            def image_points(i, s):
                dve.wait_ge(signs_done, HALVES * (i + 1))
                need(dve, m0_done, HALVES * (i - SMALL + 1))
                sg = signs[:, s % 2]
                pt = points[:, s % SMALL]
                nc.vector.tensor_tensor(pt[:, :, 0:H].rearrange("p h a b -> p h (a b)"), sg[:, :, 0:H * PW],
                                        sg[:, :, 2 * PW:(H + 2) * PW], ALU.subtract).then_inc(points_done, 1)
                pairs = sg[:, :, PW:(H + 1) * PW].rearrange("p h (t r b) -> p h t r b", r=2, b=PW)
                r1, r2 = pairs[:, :, :, 0], pairs[:, :, :, 1]
                nc.vector.tensor_tensor(pt[:, :, E12:E12 + TR], r1, r2, ALU.add).then_inc(points_done, 1)
                nc.vector.tensor_tensor(pt[:, :, E12 + TR:PROWS], r2, r1, ALU.subtract).then_inc(points_done, 1)

            def diff(t, k):
                h = k % HALVES
                dve.wait_ge(m2_done, t + 1)
                dve.wait_ge(m1_copied, t + 1)
                nc.vector.scalar_tensor_tensor(out=odd_part[:, k % 2], in0=even_ps[k % 4][:, 0:HALF_PIX],
                                               scalar=alpha_neg[:, h:h + 1], in1=m1_two[:, k % 2],
                                               op0=ALU.mult, op1=ALU.add).then_inc(diff_done, 1)

            def odd_output(t, k):
                s, h = divmod(k, HALVES)
                dve.wait_ge(m3_done, t + 1)
                dve.wait_ge(odd_part_done, t + 1)
                nc.vector.scalar_tensor_tensor(
                    out=rows_of(s, h, 1), in0=odd_ps[k % 2][:, 0:HALF_PIX].rearrange("p (a b) -> p a b", b=W),
                    scalar=alpha_sb[:, h:h + 1], in1=odd_part[:, k % 2].rearrange("p (a b) -> p a b", b=W),
                    op0=ALU.mult, op1=ALU.add).then_inc(odd_out, 1)

            def even_output(t, k):
                s, h = divmod(k, HALVES)
                dve.wait_ge(m0_done, t + 1)
                nc.vector.scalar_tensor_tensor(
                    out=rows_of(s, h, 0), in0=even_ps[k % 4][:, 0:HALF_PIX].rearrange("p (a b) -> p a b", b=W),
                    scalar=alpha_sb[:, h:h + 1], in1=rows_of(s, h, 0),
                    op0=ALU.mult, op1=ALU.add).then_inc(even_out, 1)

            for s in range(STAT_LEAD):
                sums(0, s)
            for s in range(SIGN_LEAD):
                reciprocal_std(s, s)
            image_points(0, 0)
            dve.wait_ge(alpha_ready, 2)

            def body(i0, first, last):
                for k in range(BODY * HALVES):
                    s, h = divmod(k, HALVES)
                    t = i0 * HALVES + k
                    if not (first and k == 0):
                        diff(t - 1, (k - 1) % (BODY * HALVES))
                    if h == 0:
                        if s + POINT_LEAD < BODY or not last:
                            image_points(i0 + s + POINT_LEAD, (s + POINT_LEAD) % BODY)
                        if s + SIGN_LEAD < BODY or not last:
                            reciprocal_std(i0 + s + SIGN_LEAD, (s + SIGN_LEAD) % BODY)
                    before = (t - 1, (k - 1) % (BODY * HALVES))
                    if h == 1 and (s + STAT_LEAD < BODY or not last):
                        i = i0 if s + STAT_LEAD < BODY else i0 + BODY
                        sums(i, (s + STAT_LEAD) % BODY, lambda: odd_output(*before), lambda: even_output(*before))
                    elif not (first and k == 0):
                        odd_output(*before)
                        even_output(*before)

            body(0, True, False)
            with dve.Fori(BODY, N - 2 * BODY + 1, BODY) as i0:
                body(i0, False, False)
            body(N - BODY, False, True)
            diff(TILES - 1, BODY * HALVES - 1)
            odd_output(TILES - 1, BODY * HALVES - 1)
            even_output(TILES - 1, BODY * HALVES - 1)


_INS = ['x', 'L0_conv_M', 'L0_conv_Z', 'L0_conv_alpha', 'L0_conv_rv']


def kernel(**inputs):
    import numpy as _np
    import concourse.bacc as _bacc
    from concourse import mybir as _mybir
    from concourse.bass_utils import run_bass_kernel_spmd as _run

    nc = _bacc.Bacc("TRN2", target_bir_lowering=False, num_devices=1)
    arrays, args = {}, []
    for name in _INS:
        a = _np.ascontiguousarray(inputs[name])
        arrays[f"in_{name}_dram"] = a
        args.append(nc.dram_tensor(f"in_{name}_dram", a.shape, _mybir.dt.from_np(a.dtype), kind="ExternalInput").ap())
    args.append(nc.dram_tensor("out_0_dram", inputs["x"].shape, _mybir.dt.float32, kind="ExternalOutput").ap())
    conv_preact(nc, *args)
    r = _run(nc, [arrays], core_ids=[0])
    return r.results[0]["out_0_dram"]
```

```python
from contextlib import ExitStack

import concourse.bass as bass
from concourse import mybir

P = 128
ALU = mybir.AluOpType
ACT = mybir.ActivationFunctionType
BF16 = mybir.dt.bfloat16
F32 = mybir.dt.float32

GROUPS = 32
GN_EPS = 1e-5
Z_SCALE = 100.0

BODY = 8
LOAD_LEAD = 6
STAT_LEAD = 4
GROUP_LEAD = 3
SIGN_LEAD = 2
POINT_LEAD = 1
ZR = 4
SQ = 3
QR = 6
SMALL = 4


def conv_preact(nc, x, M, Z, alpha, rv, out):
    N, C, H, W = x.shape
    K, CO, CI, KH, KW = Z.shape
    HALVES = C // P
    assert H == W and HALVES == 2 and CO == C and CI == C and N % BODY == 0 and KH == 3 and KW == 3
    PIX = H * W
    TR = H // 2
    HALF_PIX = TR * W
    PH, PW = H + 2, W + 2
    TAPS = KH * KW
    CB = 32
    CHUNKS_PER_HALF = CI // CB
    CHUNKS = HALVES * CHUNKS_PER_HALF
    CW = CB * TAPS
    CPG = C // GROUPS
    TILES = N * HALVES
    PARTS = CHUNKS_PER_HALF // HALVES
    INV_LAG = 2
    SIGN_LAG = 4
    TAPS_LAG = SIGN_LAG + 2
    WT_ROUNDS = HALVES * HALVES
    CONST_STEPS = 3 * 2 + 3
    E12 = H
    PROWS = H + 2 * TR

    x_v = x.rearrange("n (h p) a b -> n p h (a b)", p=P)
    out_v = out.rearrange("n (h p) a b -> n p h (a b)", p=P)
    z_v = Z.rearrange("k o i a b -> o k (i a b)")
    m_v = M.rearrange("o i a b -> o (i a b)")
    alpha_v = alpha.rearrange("(h p) a b -> h p (a b)", p=P)

    with ExitStack() as ctx:
        def sb(name, shape, dt):
            return ctx.enter_context(nc.sbuf_tensor(name, shape, dt))

        def psum(name, shape, dt):
            return ctx.enter_context(nc.psum_tensor(name, shape, dt))

        def sem(name):
            return ctx.enter_context(nc.semaphore(name))

        x_sb = sb("x_sb", [P, BODY, HALVES, PIX], F32)
        signs = sb("signs", [P, 2, HALVES, PH * PW], BF16)
        points = sb("points", [P, SMALL, HALVES, PROWS, PW], BF16)
        u = sb("u", [P, HALVES, 4, KW, CO], BF16)
        z_sb = sb("z_sb", [P, ZR, K, CW], F32)
        m_sb = sb("m_sb", [P, ZR, CW], F32)
        z_sq = sb("z_sq", [P, SQ, K, CW], F32)
        m_sq = sb("m_sq", [P, SQ, CW], F32)
        inv = sb("inv", [P, QR, CW], F32)
        q = sb("q", [P, QR, CW], F32)
        w_sign = sb("w_sign", [P, 2, PARTS * CW], BF16)
        g_half = sb("g_half", [P, 2, KH, P], BF16)
        g_sum = sb("g_sum", [P, 2, P], BF16)
        rv_sb = sb("rv_sb", [P, K], F32)
        alpha_sb = sb("alpha_sb", [P, HALVES], F32)
        alpha_neg = sb("alpha_neg", [P, HALVES], F32)
        alpha_two = sb("alpha_two", [P, HALVES], F32)
        ident = sb("ident", [P, P], BF16)
        one = sb("one", [P, P], F32)
        hundredth = sb("hundredth", [P, P], F32)
        average = sb("average", [P, P], F32)
        unread = sb("unread", [P, 2, PIX], BF16)
        bn = sb("bn", [P, 2, 2, 6], F32)
        chan = sb("chan", [P, SMALL, 4], F32)
        grp = sb("grp", [P, SMALL, 4], F32)
        mean_sq = sb("mean_sq", [P, SMALL, 2], F32)
        var = sb("var", [P, SMALL, 2], F32)
        var_eps = sb("var_eps", [P, SMALL, 2], F32)
        rstd = sb("rstd", [P, SMALL, 2], F32)
        shift = sb("shift", [P, SMALL, 2], F32)
        m1_two = sb("m1_two", [P, 2, HALF_PIX], F32)
        odd_part = sb("odd_part", [P, 2, HALF_PIX], F32)

        even_ps = [psum(f"even_ps{i}", [P, 512], F32) for i in range(4)]
        odd_ps = [psum(f"odd_ps{i}", [P, 512], F32) for i in range(2)]
        grp_ps = psum("grp_ps", [P, 512], F32)
        wt_ps = psum("wt_ps", [P, 1024], BF16)
        taps_ps = [wt_ps[:, 0:KH * P]] + [odd_ps[i][:].bitcast(BF16)[:, 0:KH * P] for i in range(KW - 1)]

        consts_loaded = sem("consts_loaded")
        z_loaded = [sem(f"z_loaded{i}") for i in range(ZR)]
        x_loaded = [sem(f"x_loaded{i}") for i in range(BODY)]
        stored = [sem(f"stored{i}") for i in range(BODY)]
        const_step = sem("const_step")
        borders_zero = sem("borders_zero")
        alpha_ready = sem("alpha_ready")
        pool_step = sem("pool_step")
        z_squares_done = sem("z_squares_done")
        m_squares_done = sem("m_squares_done")
        fold_done = sem("fold_done")
        q_step = sem("q_step")
        q_done = sem("q_done")
        a_done = sem("a_done")
        inv_done = sem("inv_done")
        w_done = sem("w_done")
        w_sign_done = sem("w_sign_done")
        wt_done = sem("wt_done")
        g_done = sem("g_done")
        g_half_done = sem("g_half_done")
        u_done = sem("u_done")
        act_sums_done = sem("act_sums_done")
        dve_sums_done = sem("dve_sums_done")
        bn_step = sem("bn_step")
        grp_done = sem("grp_done")
        grp_copied = sem("grp_copied")
        var_step = sem("var_step")
        var_done = sem("var_done")
        rstd_done = sem("rstd_done")
        shift_done = sem("shift_done")
        signs_done = sem("signs_done")
        points_done = sem("points_done")
        m1_done = sem("m1_done")
        m2_done = sem("m2_done")
        m3_done = sem("m3_done")
        m0_done = sem("m0_done")
        m1_copied = sem("m1_copied")
        diff_done = sem("diff_done")
        odd_part_done = sem("odd_part_done")
        odd_out = sem("odd_out")
        even_out = sem("even_out")

        def need(eng, s, value):
            if not (isinstance(value, int) and value <= 0):
                eng.wait_ge(s, value)

        def rows_of(slot, h, parity):
            return x_sb[:, slot, h, :].rearrange("p (t r w) -> p t r w", r=2, w=W)[:, :, parity, :]

        block = ctx.enter_context(nc.Block())

        @block.sync
        def _(sp):
            sp.dma_start(rv_sb[:], rv.to_broadcast([P, K])).then_inc(consts_loaded, 16)
            for h in range(HALVES):
                sp.dma_start(alpha_sb[:, h:h + 1], alpha_v[h]).then_inc(consts_loaded, 16)

            def load_chunk(c):
                h, b = divmod(c, CHUNKS_PER_HALF)
                need(sp, q_done, c - ZR + 1)
                need(sp, z_squares_done, c - ZR + 1)
                need(sp, m_squares_done, c - ZR + 1)
                sp.dma_start(z_sb[:, c % ZR], z_v[h * P:(h + 1) * P, :, b * CW:(b + 1) * CW]).then_inc(z_loaded[c % ZR], 16)
                sp.dma_start(m_sb[:, c % ZR], m_v[h * P:(h + 1) * P, b * CW:(b + 1) * CW]).then_inc(z_loaded[c % ZR], 16)

            def load(i0, s, first):
                if not first:
                    sp.wait_ge(stored[s], i0 * 2)
                sp.dma_start(x_sb[:, s], x_v[i0 + s]).then_inc(x_loaded[s], 16)

            def store(i0, s):
                sp.wait_ge(odd_out, (i0 + s + 1) * HALVES)
                sp.wait_ge(even_out, (i0 + s + 1) * HALVES)
                sp.dma_start(out_v[i0 + s], x_sb[:, s]).then_inc(stored[s], 16)

            for c in range(CHUNKS):
                load_chunk(c)
                if c == CHUNKS - 5:
                    load(0, 0, True)
            for s in range(1, LOAD_LEAD):
                load(0, s, True)

            def body(i0, first, last):
                for s in range(BODY):
                    store(i0, s)
                    t = s + LOAD_LEAD
                    if t < BODY:
                        load(i0, t, first)
                    elif not last:
                        load(i0 + BODY, t - BODY, False)

            body(0, True, False)
            with sp.Fori(BODY, N - 2 * BODY + 1, BODY) as i0:
                body(i0, False, False)
            body(N - BODY, False, True)
            for s in range(BODY):
                sp.wait_ge(stored[s], 16 * (N // BODY))

        @block.tensor
        def _(pe):
            def chunk_a(c):
                pe.wait_ge(fold_done, c + 1)
                need(pe, inv_done, c - 3)
                for k in range(K // 2):
                    pe.matmul(even_ps[c % 4][:, 0:CW], hundredth[:], z_sq[:, c % SQ, k], start=k == 0, stop=False)
                pe.wait_ge(m_squares_done, c + 1)
                pe.matmul(even_ps[c % 4][:, 0:CW], one[:], m_sq[:, c % SQ], start=False, stop=True).then_inc(a_done, 1)

            def transpose_weights(g):
                pe.wait_ge(w_sign_done, PARTS * (g + 1))
                v = w_sign[:, g % 2].rearrange("p (i a b) -> p a b i", a=KH, b=KW)
                for kw in range(KW):
                    need(pe, g_done, 2 * KW * g)
                    need(pe, g_half_done, KW * g)
                    for kh in range(KH):
                        mm = pe.transpose(taps_ps[kw][:, kh * P:(kh + 1) * P], v[:, kh, kw, :], ident[:])
                    mm.then_inc(wt_done, 1)

            def group(i, k):
                pe.wait_ge(act_sums_done, 2 * (i + 1))
                pe.wait_ge(dve_sums_done, i + 1)
                need(pe, grp_copied, i)
                pe.matmul(grp_ps[:, 0:4], average[:], chan[:, k % SMALL], start=True, stop=True).then_inc(grp_done, 1)

            def product(bank, point, row0, step, s, h, start, stop):
                for ch in range(HALVES):
                    for kw in range(KW):
                        e = points[:, s % SMALL, ch, row0:row0 + step * (TR - 1) + 1:step, kw:kw + W]
                        mm = pe.matmul(bank[:, 0:HALF_PIX], u[:, ch, point, kw, h * P:(h + 1) * P], e,
                                       start=start and ch == 0 and kw == 0,
                                       stop=stop and ch == HALVES - 1 and kw == KW - 1, skip_group_check=True)
                return mm

            def finish(t, k):
                s, h = divmod(k, HALVES)
                need(pe, odd_out, t - 1)
                product(odd_ps[k % 2], 3, 1, 2, s, h, True, True).then_inc(m3_done, 1)
                pe.wait_ge(diff_done, t + 1)
                product(even_ps[k % 4], 0, 0, 2, s, h, False, True).then_inc(m0_done, 1)

            pe.wait_ge(const_step, CONST_STEPS)
            for c in range(CHUNKS):
                if c == CHUNKS - 1:
                    group(0, 0)
                chunk_a(c)
                if c >= PARTS + SIGN_LAG - 1 and (c - SIGN_LAG + 1) % PARTS == 0:
                    transpose_weights((c - SIGN_LAG + 1) // PARTS - 1)
            transpose_weights(WT_ROUNDS - 1)
            group(1, 1)
            pe.wait_ge(u_done, 2 * HALVES * HALVES * KW)
            pe.wait_ge(g_done, 2 * HALVES * HALVES * KW)

            def body(i0, first, last):
                for k in range(BODY * HALVES):
                    s, h = divmod(k, HALVES)
                    i, t = i0 + s, i0 * HALVES + k
                    if h == 0:
                        pe.wait_ge(points_done, (i + 1) * 3)
                    need(pe, even_out, t - 3)
                    product(even_ps[k % 4], 1, E12, 1, s, h, True, False).then_inc(m1_done, 1)
                    if first and k == 0:
                        group(2, 2)
                    else:
                        finish(t - 1, (k - 1) % (BODY * HALVES))
                    pe.wait_ge(m1_copied, t + 1)
                    product(even_ps[k % 4], 2, E12 + TR, 1, s, h, False, False).then_inc(m2_done, 1)
                    if h == 0 and not (last and s + GROUP_LEAD >= BODY):
                        group(i + GROUP_LEAD, s + GROUP_LEAD)

            body(0, True, False)
            with pe.Fori(BODY, N - 2 * BODY + 1, BODY) as i0:
                body(i0, False, False)
            body(N - BODY, False, True)
            finish(TILES - 1, BODY * HALVES - 1)

        @block.scalar
        def _(act):
            def chunk_squares(c):
                act.wait_ge(z_loaded[c % ZR], 32 * (c // ZR + 1))
                need(act, a_done, c - SQ + 1)
                nc.scalar.activation(z_sq[:, c % SQ], z_sb[:, c % ZR], ACT.Square).then_inc(z_squares_done, 1)

            def chunk_inv(c):
                act.wait_ge(a_done, c + 1)
                need(act, w_done, c - QR + 1)
                nc.scalar.activation(inv[:, c % QR], even_ps[c % 4][:, 0:CW],
                                     ACT.Abs_reciprocal_sqrt).then_inc(inv_done, 1)

            def chunk_sign(c):
                act.wait_ge(w_done, c + 1)
                g, part = divmod(c, PARTS)
                need(act, wt_done, KW * (g - 1))
                nc.scalar.activation(w_sign[:, g % 2, part * CW:(part + 1) * CW], q[:, c % QR],
                                     ACT.Sign).then_inc(w_sign_done, 1)

            def copy_taps(r):
                g, kw = divmod(r, KW)
                h, ch = divmod(g, HALVES)
                act.wait_ge(g_half_done, r + 1)
                nc.scalar.activation(u[:, ch, 0, kw, h * P:(h + 1) * P], taps_ps[kw][:, 0:P], ACT.Copy).then_inc(g_done, 1)
                nc.scalar.activation(u[:, ch, 3, kw, h * P:(h + 1) * P], taps_ps[kw][:, 2 * P:3 * P],
                                     ACT.Copy, scale=-1.0).then_inc(g_done, 1)

            def sums(i0, s):
                act.wait_ge(x_loaded[s], (i0 + BODY) * 2)
                need(act, act_sums_done, (i0 + s) * 2)
                nc.scalar.activation(unread[:, 0], x_sb[:, s, 0], ACT.Copy, scale=1.0 / PIX,
                                     accum_out=chan[:, s % SMALL, 0:1]).then_inc(act_sums_done, 1)
                nc.scalar.activation(unread[:, 1], x_sb[:, s, 0], ACT.Square, scale=1.0 / W,
                                     accum_out=chan[:, s % SMALL, 1:2]).then_inc(act_sums_done, 1)

            def copy_group(i, s):
                act.wait_ge(grp_done, i + 1)
                nc.scalar.activation(grp[:, s % SMALL], grp_ps[:, 0:4], ACT.Copy).then_inc(grp_copied, 1)

            def deviation(i, s):
                act.wait_ge(var_done, i + 1)
                nc.scalar.activation(rstd[:, s % SMALL], var_eps[:, s % SMALL],
                                     ACT.Abs_reciprocal_sqrt).then_inc(rstd_done, 1)

            def image_signs(i, s):
                act.wait_ge(shift_done, i + 1)
                need(act, points_done, 3 * (i - 1))
                for h in range(HALVES):
                    o = signs[:, s % 2, h].rearrange("p (a b) -> p a b", b=PW)[:, 1:H + 1, 1:W + 1]
                    nc.scalar.activation(o, x_sb[:, s, h].rearrange("p (a b) -> p a b", b=W), ACT.Sign,
                                         bias=shift[:, s % SMALL, h:h + 1],
                                         scale=rstd[:, s % SMALL, h:h + 1]).then_inc(signs_done, 1)

            def copy_column_taps(g):
                for kw in range(KW):
                    copy_taps(g * KW + kw)

            for c in range(CHUNKS):
                chunk_squares(c)
                if c >= INV_LAG:
                    chunk_inv(c - INV_LAG)
                if c >= SIGN_LAG:
                    chunk_sign(c - SIGN_LAG)
                if c >= PARTS + TAPS_LAG and (c - TAPS_LAG) % PARTS == 0:
                    copy_column_taps((c - TAPS_LAG) // PARTS - 1)
                if c == CHUNKS - 4:
                    sums(0, 0)
            copy_group(0, 0)
            chunk_inv(CHUNKS - 2)
            deviation(0, 0)
            chunk_sign(CHUNKS - 4)
            sums(0, 1)
            chunk_inv(CHUNKS - 1)
            chunk_sign(CHUNKS - 3)
            copy_column_taps(WT_ROUNDS - 2)
            chunk_sign(CHUNKS - 2)
            chunk_sign(CHUNKS - 1)
            act.wait_ge(borders_zero, 1)
            image_signs(0, 0)
            copy_column_taps(WT_ROUNDS - 1)
            copy_group(1, 1)
            deviation(1, 1)
            sums(0, 2)
            act.wait_ge(alpha_ready, 2)

            def body(i0, first, last):
                def lead(f, s, ahead):
                    if s + ahead < BODY or not last:
                        f(i0 + s + ahead, (s + ahead) % BODY)

                for k in range(BODY * HALVES):
                    s, h = divmod(k, HALVES)
                    t = i0 * HALVES + k
                    act.wait_ge(m1_done, t + 1)
                    need(act, diff_done, t - 1)
                    nc.scalar.activation(m1_two[:, k % 2], even_ps[k % 4][:, 0:HALF_PIX], ACT.Copy,
                                         scale=alpha_two[:, h:h + 1]).then_inc(m1_copied, 1)
                    if first and k == 0:
                        image_signs(1, 1)
                        copy_group(2, 2)
                        sums(0, 3)
                    if h == 0:
                        lead(deviation, s, SIGN_LEAD)
                        if s + STAT_LEAD < BODY:
                            sums(i0, s + STAT_LEAD)
                        elif not last:
                            sums(i0 + BODY, s + STAT_LEAD - BODY)
                    else:
                        lead(copy_group, s, GROUP_LEAD)
                        lead(image_signs, s, SIGN_LEAD)

            body(0, True, False)
            with act.Fori(BODY, N - 2 * BODY + 1, BODY) as i0:
                body(i0, False, False)
            body(N - BODY, False, True)

        @block.gpsimd
        def _(pool):
            made = [0]

            def after(ins):
                made[0] += 1
                ins.then_inc(const_step, 1)
                pool.wait_ge(const_step, made[0])

            after(nc.gpsimd.memset(ident[:], 0.0))
            after(nc.gpsimd.affine_select(out=ident[:], in_=ident[:], compare_op=ALU.not_equal, fill=1.0, base=0,
                                          pattern=[[-1, P]], channel_multiplier=1))
            for diag, value in ((one, 1.0), (hundredth, 1.0 / Z_SCALE)):
                after(nc.gpsimd.memset(diag[:], 0.0))
                after(nc.gpsimd.affine_select(out=diag[:], in_=diag[:], compare_op=ALU.not_equal, fill=value, base=0,
                                              pattern=[[-1, P]], channel_multiplier=1))
            v = average[:].rearrange("p (g c) -> p g c", c=CPG)
            after(nc.gpsimd.memset(average[:], 1.0 / CPG))
            after(nc.gpsimd.affine_select(out=v, in_=v, compare_op=ALU.is_ge, fill=0.0, base=0,
                                          pattern=[[-CPG, P // CPG], [0, CPG]], channel_multiplier=1))
            after(nc.gpsimd.affine_select(out=v, in_=v, compare_op=ALU.is_ge, fill=0.0, base=CPG - 1,
                                          pattern=[[CPG, P // CPG], [0, CPG]], channel_multiplier=-1))
            nc.gpsimd.memset(signs[:], 0.0).then_inc(borders_zero, 1)

            steps = [0]

            def then(ins):
                steps[0] += 1
                ins.then_inc(pool_step, 1)
                pool.wait_ge(pool_step, steps[0])

            def chunk_fold(c):
                pool.wait_ge(z_loaded[c % ZR], 32 * (c // ZR + 1))
                need(pool, a_done, c - SQ + 1)
                nc.gpsimd.tensor_tensor(m_sq[:, c % SQ], m_sb[:, c % ZR], m_sb[:, c % ZR],
                                        ALU.mult).then_inc(m_squares_done, 1)
                pool.wait_ge(z_squares_done, c + 1)
                nc.gpsimd.tensor_tensor(z_sq[:, c % SQ, 0:K // 2], z_sq[:, c % SQ, 0:K // 2],
                                        z_sq[:, c % SQ, K // 2:K], ALU.add).then_inc(fold_done, 1)

            def combine_taps(r):
                g, kw = divmod(r, KW)
                h, ch = divmod(g, HALVES)
                pool.wait_ge(g_half_done, r + 1)
                then(nc.gpsimd.tensor_tensor(g_sum[:, r % 2], g_half[:, r % 2, 0], g_half[:, r % 2, 2], ALU.add))
                for point, op in ((1, ALU.add), (2, ALU.subtract)):
                    nc.gpsimd.tensor_tensor(u[:, ch, point, kw, h * P:(h + 1) * P], g_sum[:, r % 2],
                                            g_half[:, r % 2, 1], op).then_inc(u_done, 1)

            def combine_column_taps(g):
                for kw in range(KW):
                    combine_taps(g * KW + kw)

            for c in range(CHUNKS):
                chunk_fold(c)
                if c >= PARTS + TAPS_LAG and (c - TAPS_LAG) % PARTS == 0:
                    combine_column_taps((c - TAPS_LAG) // PARTS - 1)

            def variance(i, s, between=None):
                pool.wait_ge(grp_copied, i + 1)
                k = s % SMALL
                n = i * 2
                mean = grp[:, k, 0:4:2]
                nc.gpsimd.tensor_tensor(mean_sq[:, k], mean, mean, ALU.mult).then_inc(var_step, 1)
                pool.wait_ge(var_step, n + 1)
                nc.gpsimd.tensor_tensor(var[:, k], grp[:, k, 1:4:2], mean_sq[:, k], ALU.subtract).then_inc(var_step, 1)
                pool.wait_ge(var_step, n + 2)
                if between:
                    between()
                nc.gpsimd.tensor_scalar(var_eps[:, k], var[:, k], 0.0, GN_EPS, ALU.max, ALU.add).then_inc(var_done, 1)

            def odd(t, k):
                s, h = divmod(k, HALVES)
                v = odd_part[:, k % 2].rearrange("p (a b) -> p a b", b=W)
                pool.wait_ge(diff_done, t + 1)
                nc.gpsimd.tensor_tensor(v, v, rows_of(s, h, 1), ALU.add).then_inc(odd_part_done, 1)

            variance(0, 0)
            combine_column_taps(WT_ROUNDS - 2)
            combine_column_taps(WT_ROUNDS - 1)
            variance(1, 1)
            variance(2, 2)

            def body(i0, first, last):
                for k in range(BODY * HALVES):
                    s, h = divmod(k, HALVES)

                    def odd_before():
                        if not (first and k == 0):
                            odd(i0 * HALVES + k - 1, (k - 1) % (BODY * HALVES))

                    if h == 1 and (s + GROUP_LEAD < BODY or not last):
                        variance(i0 + s + GROUP_LEAD, (s + GROUP_LEAD) % BODY, odd_before)
                    else:
                        odd_before()

            body(0, True, False)
            with pool.Fori(BODY, N - 2 * BODY + 1, BODY) as i0:
                body(i0, False, False)
            body(N - BODY, False, True)
            odd(TILES - 1, BODY * HALVES - 1)

        @block.vector
        def _(dve):
            dve.wait_ge(consts_loaded, 16 * (1 + HALVES))
            nc.vector.tensor_scalar(alpha_neg[:], alpha_sb[:], -1.0, None, ALU.mult).then_inc(alpha_ready, 1)
            nc.vector.tensor_scalar(alpha_two[:], alpha_sb[:], 2.0, None, ALU.mult).then_inc(alpha_ready, 1)

            def chunk_pair_q(c):
                for k in range(K):
                    for d in (c, c + 1):
                        if k == 0:
                            dve.wait_ge(z_loaded[d % ZR], 32 * (d // ZR + 1))
                            need(dve, w_sign_done, d - QR + 1)
                        else:
                            dve.wait_ge(q_step, d // 2 * 2 * (K - 1) + 2 * (k - 1) + d % 2 + 1)
                        nc.vector.scalar_tensor_tensor(
                            out=q[:, d % QR], in0=z_sb[:, d % ZR, k], scalar=rv_sb[:, k:k + 1],
                            in1=m_sb[:, d % ZR] if k == 0 else q[:, d % QR], op0=ALU.mult,
                            op1=ALU.add).then_inc(q_step if k < K - 1 else q_done, 1)

            def chunk_w(c):
                dve.wait_ge(inv_done, c + 1)
                dve.wait_ge(q_done, c + 1)
                nc.vector.tensor_tensor(q[:, c % QR], q[:, c % QR], inv[:, c % QR], ALU.mult).then_inc(w_done, 1)

            def halve_taps(r):
                dve.wait_ge(wt_done, r + 1)
                need(dve, u_done, 2 * (r - 1))
                nc.vector.tensor_scalar(g_half[:, r % 2].rearrange("p a o -> p (a o)"), taps_ps[r % KW],
                                        0.5, None, ALU.mult).then_inc(g_half_done, 1)

            def sums(i0, s, first_output=None, second_output=None):
                dve.wait_ge(x_loaded[s], (i0 + BODY) * 2)
                b, k = s % 2, s % SMALL
                n = (i0 + s) * 3
                for c in range(2):
                    nc.vector.bn_stats(bn[:, b, c], x_sb[:, s, 1, c * HALF_PIX:(c + 1) * HALF_PIX]).then_inc(bn_step, 1)
                dve.wait_ge(bn_step, n + 2)
                if first_output:
                    first_output()
                nc.vector.bn_aggr(chan[:, k, 2:4], bn[:, b].rearrange("p c k -> p (c k)")).then_inc(bn_step, 1)
                dve.wait_ge(bn_step, n + 3)
                if second_output:
                    second_output()
                nc.vector.scalar_tensor_tensor(out=chan[:, k, 3:4], in0=chan[:, k, 2:3],
                                               scalar=chan[:, k, 2:3], in1=chan[:, k, 3:4],
                                               op0=ALU.mult, op1=ALU.add).then_inc(dve_sums_done, 1)

            def negative_mean(i, s):
                dve.wait_ge(rstd_done, i + 1)
                k = s % SMALL
                nc.vector.scalar_tensor_tensor(out=shift[:, k], in0=grp[:, k, 0:4:2], scalar=-1.0,
                                               in1=rstd[:, k], op0=ALU.mult, op1=ALU.mult).then_inc(shift_done, 1)

            def image_points(i, s):
                dve.wait_ge(signs_done, HALVES * (i + 1))
                need(dve, m0_done, HALVES * (i - SMALL + 1))
                sg = signs[:, s % 2]
                pt = points[:, s % SMALL]
                nc.vector.tensor_tensor(pt[:, :, 0:H].rearrange("p h a b -> p h (a b)"), sg[:, :, 0:H * PW],
                                        sg[:, :, 2 * PW:(H + 2) * PW], ALU.subtract).then_inc(points_done, 1)
                pairs = sg[:, :, PW:(H + 1) * PW].rearrange("p h (t r b) -> p h t r b", r=2, b=PW)
                r1, r2 = pairs[:, :, :, 0], pairs[:, :, :, 1]
                nc.vector.tensor_tensor(pt[:, :, E12:E12 + TR], r1, r2, ALU.add).then_inc(points_done, 1)
                nc.vector.tensor_tensor(pt[:, :, E12 + TR:PROWS], r2, r1, ALU.subtract).then_inc(points_done, 1)

            def diff(t, k):
                h = k % HALVES
                dve.wait_ge(m2_done, t + 1)
                dve.wait_ge(m1_copied, t + 1)
                nc.vector.scalar_tensor_tensor(out=odd_part[:, k % 2], in0=even_ps[k % 4][:, 0:HALF_PIX],
                                               scalar=alpha_neg[:, h:h + 1], in1=m1_two[:, k % 2],
                                               op0=ALU.mult, op1=ALU.add).then_inc(diff_done, 1)

            def odd_output(t, k):
                s, h = divmod(k, HALVES)
                dve.wait_ge(m3_done, t + 1)
                dve.wait_ge(odd_part_done, t + 1)
                nc.vector.scalar_tensor_tensor(
                    out=rows_of(s, h, 1), in0=odd_ps[k % 2][:, 0:HALF_PIX].rearrange("p (a b) -> p a b", b=W),
                    scalar=alpha_sb[:, h:h + 1], in1=odd_part[:, k % 2].rearrange("p (a b) -> p a b", b=W),
                    op0=ALU.mult, op1=ALU.add).then_inc(odd_out, 1)

            def even_output(t, k):
                s, h = divmod(k, HALVES)
                dve.wait_ge(m0_done, t + 1)
                nc.vector.scalar_tensor_tensor(
                    out=rows_of(s, h, 0), in0=even_ps[k % 4][:, 0:HALF_PIX].rearrange("p (a b) -> p a b", b=W),
                    scalar=alpha_sb[:, h:h + 1], in1=rows_of(s, h, 0),
                    op0=ALU.mult, op1=ALU.add).then_inc(even_out, 1)

            def halve_column_taps(g):
                for kw in range(KW):
                    halve_taps(g * KW + kw)

            for c in range(0, CHUNKS, 2):
                chunk_pair_q(c)
                if c >= 2:
                    chunk_w(c - 2)
                    chunk_w(c - 1)
                if c >= 2 * PARTS and c % PARTS == 0:
                    halve_column_taps(c // PARTS - 2)
                if c == CHUNKS - 4:
                    sums(0, 0)
            sums(0, 1)
            negative_mean(0, 0)
            chunk_w(CHUNKS - 2)
            halve_column_taps(WT_ROUNDS - 2)
            chunk_w(CHUNKS - 1)
            halve_column_taps(WT_ROUNDS - 1)
            image_points(0, 0)
            sums(0, 2)
            negative_mean(1, 1)
            sums(0, 3)
            dve.wait_ge(alpha_ready, 2)

            def body(i0, first, last):
                for k in range(BODY * HALVES):
                    s, h = divmod(k, HALVES)
                    t = i0 * HALVES + k
                    if not (first and k == 0):
                        diff(t - 1, (k - 1) % (BODY * HALVES))
                    if h == 0:
                        if s + POINT_LEAD < BODY or not last:
                            image_points(i0 + s + POINT_LEAD, (s + POINT_LEAD) % BODY)
                        if s + SIGN_LEAD < BODY or not last:
                            negative_mean(i0 + s + SIGN_LEAD, (s + SIGN_LEAD) % BODY)
                    before = (t - 1, (k - 1) % (BODY * HALVES))
                    if h == 1 and (s + STAT_LEAD < BODY or not last):
                        i = i0 if s + STAT_LEAD < BODY else i0 + BODY
                        sums(i, (s + STAT_LEAD) % BODY, lambda: odd_output(*before), lambda: even_output(*before))
                    elif not (first and k == 0):
                        odd_output(*before)
                        even_output(*before)

            body(0, True, False)
            with dve.Fori(BODY, N - 2 * BODY + 1, BODY) as i0:
                body(i0, False, False)
            body(N - BODY, False, True)
            diff(TILES - 1, BODY * HALVES - 1)
            odd_output(TILES - 1, BODY * HALVES - 1)
            even_output(TILES - 1, BODY * HALVES - 1)


_INS = ['x', 'L0_conv_M', 'L0_conv_Z', 'L0_conv_alpha', 'L0_conv_rv']


def kernel(**inputs):
    import numpy as _np
    import concourse.bacc as _bacc
    from concourse import mybir as _mybir
    from concourse.bass_utils import run_bass_kernel_spmd as _run

    nc = _bacc.Bacc("TRN2", target_bir_lowering=False, num_devices=1)
    arrays, args = {}, []
    for name in _INS:
        a = _np.ascontiguousarray(inputs[name])
        arrays[f"in_{name}_dram"] = a
        args.append(nc.dram_tensor(f"in_{name}_dram", a.shape, _mybir.dt.from_np(a.dtype), kind="ExternalInput").ap())
    args.append(nc.dram_tensor("out_0_dram", inputs["x"].shape, _mybir.dt.float32, kind="ExternalOutput").ap())
    conv_preact(nc, *args)
    r = _run(nc, [arrays], core_ids=[0])
    return r.results[0]["out_0_dram"]
```
